# Optimizing a Trainium2 kernel written in Bass

```python
import numpy as np
import jax
import jax.numpy as jnp

def _softmax(x, axis=-1):
    return jax.nn.softmax(x, axis=axis)

def _gelu(x):
    return jax.nn.gelu(x, approximate=True)

def _silu(x):
    return jax.nn.silu(x)

def _sigmoid(x):
    return jax.nn.sigmoid(x)

def _layernorm(x, axis=-1, eps=1e-05):
    m = jnp.mean(x, axis=axis, keepdims=True)
    v = jnp.var(x, axis=axis, keepdims=True)
    return (x - m) / jnp.sqrt(v + eps)

def _scatter_add(tgt, idx, src, axis=0):
    return tgt.at[idx].add(src)

def _segment_sum(src, seg, n):
    return jax.ops.segment_sum(src, seg, n)
kernel_name = 'mk_hybrid_d1_jaxref_r8_b53eef'

def setup_inputs(seed: int=0):
    np.random.seed(seed)
    _w = jnp.asarray

    def _L0_attn_a_setup():
        import jax, jax.numpy as jnp
        import numpy as np
        B, S, D, H, F = (4, 1024, 128, 16, 64)
        DK = D // H
        EPS = 1e-06

        def _heads(x, W, b):
            y = jnp.einsum('bsd,de->bse', x, W) + b
            return y.reshape(x.shape[0], x.shape[1], H, DK).transpose(0, 2, 1, 3)
        key = jax.random.key(seed)
        ks = jax.random.split(key, 6)
        scale = 1.0 / np.sqrt(D)
        x = jax.random.normal(ks[0], (B, S, D), dtype=jnp.float32)
        Wq = jax.random.normal(ks[1], (D, D), dtype=jnp.float32) * scale
        Wk = jax.random.normal(ks[2], (D, D), dtype=jnp.float32) * scale
        Wv = jax.random.normal(ks[3], (D, D), dtype=jnp.float32) * scale
        Wo = jax.random.normal(ks[4], (D, D), dtype=jnp.float32) * scale
        rw = jax.random.normal(ks[5], (H, DK, F), dtype=jnp.float32) / np.sqrt(DK)
        zb = jnp.zeros((D,), dtype=jnp.float32)
        return {'x': x, 'Wq': Wq, 'bq': zb, 'Wk': Wk, 'bk': zb, 'Wv': Wv, 'bv': zb, 'Wo': Wo, 'bo': zb, 'rw': rw}
    _L0_attn_a_in = _L0_attn_a_setup()

    def _L0_attn_b_setup():
        import jax, jax.numpy as jnp
        import numpy as np
        HEADS = 16
        HIDDEN = 128
        key = jax.random.key(seed)
        ks = jax.random.split(key, 9)
        E, H = (128, HIDDEN)
        N, L = (4, 256)
        s = 0.02
        return {'X_embed': jax.random.normal(ks[0], (N, L, E), dtype=jnp.float32), 'Wq': jax.random.normal(ks[1], (E, H), dtype=jnp.float32) * s, 'bq': jax.random.normal(ks[2], (H,), dtype=jnp.float32) * s, 'Wk': jax.random.normal(ks[3], (E, H), dtype=jnp.float32) * s, 'bk': jax.random.normal(ks[4], (H,), dtype=jnp.float32) * s, 'Wv': jax.random.normal(ks[5], (E, H), dtype=jnp.float32) * s, 'bv': jax.random.normal(ks[6], (H,), dtype=jnp.float32) * s, 'Wo': jax.random.normal(ks[7], (H, H), dtype=jnp.float32) * s, 'bo': jax.random.normal(ks[8], (H,), dtype=jnp.float32) * s}
    _L0_attn_b_in = _L0_attn_b_setup()

    def _L0_ffn_setup():
        import jax, jax.numpy as jnp
        import numpy as np
        DIM = 128
        DEPTH = 2
        HEADS = 8
        DIM_HEAD = 64
        WINDOW = 64
        INNER = HEADS * DIM_HEAD
        HID = int(DIM * 4 * 2 / 3)
        B, N = (2, 1024)
        QK_SCALE = 8.0

        def shift_token(t):
            t1, t2 = jnp.split(t, 2, axis=-1)
            t2 = jnp.pad(t2, ((0, 0), (1, 0), (0, 0)))[:, :-1]
            return jnp.concatenate([t1, t2], axis=-1)

        def l2norm(t):
            return t / jnp.clip(jnp.linalg.norm(t, axis=-1, keepdims=True), 1e-12)

        def rotate_half(x):
            x1, x2 = jnp.split(x, 2, axis=-1)
            return jnp.concatenate([-x2, x1], axis=-1)

        def rotary_xpos(q, k):
            n = q.shape[-2]
            half_idx = jnp.arange(0, DIM_HEAD, 2, dtype=jnp.float32)
            inv_freq = 1.0 / 10000.0 ** (half_idx / DIM_HEAD)
            t = jnp.arange(n, dtype=jnp.float32)
            freqs = t[:, None] * inv_freq[None, :]
            freqs = jnp.concatenate([freqs, freqs], axis=-1)
            base = (half_idx + 0.4 * DIM_HEAD) / (1.4 * DIM_HEAD)
            power = (t - n // 2) / float(WINDOW // 2)
            scale = base[None, :] ** power[:, None]
            scale = jnp.concatenate([scale, scale], axis=-1)
            cos, sin = (jnp.cos(freqs), jnp.sin(freqs))
            q = q * cos * scale + rotate_half(q) * sin * scale
            k = k * cos / scale + rotate_half(k) * sin / scale
            return (q, k)

        def local_attention(q, k, v):
            b, h, n, d = q.shape
            w = n // WINDOW
            bq = q.reshape(b, h, w, WINDOW, d) * QK_SCALE
            bk = k.reshape(b, h, w, WINDOW, d)
            bv = v.reshape(b, h, w, WINDOW, d)

            def look_around(t):
                p = jnp.pad(t, ((0, 0), (0, 0), (1, 0), (0, 0), (0, 0)))
                return jnp.concatenate([p[:, :, :w], p[:, :, 1:]], axis=3)
            bk, bv = (look_around(bk), look_around(bv))
            bt = jnp.arange(n).reshape(w, WINDOW)
            btp = jnp.pad(bt, ((1, 0), (0, 0)), constant_values=-1)
            btk = jnp.concatenate([btp[:w], btp[1:]], axis=1)
            sim = jnp.einsum('bhwid,bhwjd->bhwij', bq, bk)
            i = bt[:, :, None]
            j = btk[:, None, :]
            mask = (i < j) | (i > j + WINDOW) | (j == -1)
            sim = jnp.where(mask, -jnp.finfo(sim.dtype).max, sim)
            attn = jax.nn.softmax(sim, axis=-1)
            out = jnp.einsum('bhwij,bhwjd->bhwid', attn, bv)
            return out.reshape(b, h, n, d)

        def _layer(x, wqkv, qs, ksc, wo, lg, lb, w1, b1, w2, b2):
            b, n, _ = x.shape
            h = shift_token(x)
            qkv = h @ wqkv
            q, k, v = jnp.split(qkv, 3, axis=-1)
            to_heads = lambda t: t.reshape(b, n, HEADS, DIM_HEAD).transpose(0, 2, 1, 3)
            q, k, v = (to_heads(q), to_heads(k), to_heads(v))
            q = l2norm(q) * qs
            k = l2norm(k) * ksc
            q, k = rotary_xpos(q, k)
            o = local_attention(q, k, v)
            o = o.transpose(0, 2, 1, 3).reshape(b, n, INNER)
            x = x + o @ wo
            h = shift_token(x)
            mu = h.mean(-1, keepdims=True)
            var = h.var(-1, keepdims=True)
            h = (h - mu) / jnp.sqrt(var + 1e-05) * lg + lb
            h = h @ w1 + b1
            a, g = jnp.split(h, 2, axis=-1)
            h = a * jax.nn.gelu(g, approximate=False)
            x = x + h @ w2 + b2
            return x
        key = jax.random.key(seed)
        ks = jax.random.split(key, 6)
        return {'x': jax.random.normal(ks[0], (B, N, DIM), jnp.float32), 'wqkv': jax.random.normal(ks[1], (DEPTH, DIM, 3 * INNER), jnp.float32) * 0.02, 'q_scale': jnp.ones((DEPTH, DIM_HEAD), jnp.float32), 'k_scale': jnp.ones((DEPTH, DIM_HEAD), jnp.float32), 'wo': jax.random.normal(ks[2], (DEPTH, INNER, DIM), jnp.float32) * 0.02, 'ln_g': jnp.ones((DEPTH, DIM), jnp.float32), 'ln_b': jnp.zeros((DEPTH, DIM), jnp.float32), 'w1': jax.random.normal(ks[3], (DEPTH, DIM, 2 * HID), jnp.float32) * 0.02, 'b1': jnp.zeros((DEPTH, 2 * HID), jnp.float32), 'w2': jax.random.normal(ks[4], (DEPTH, HID, DIM), jnp.float32) * 0.02, 'b2': jnp.zeros((DEPTH, DIM), jnp.float32)}
    _L0_ffn_in = _L0_ffn_setup()
    _d = {'L0_attn_a_x': _L0_attn_a_in['x'], 'L0_attn_a_Wq': _L0_attn_a_in['Wq'], 'L0_attn_a_bq': _L0_attn_a_in['bq'], 'L0_attn_a_Wk': _L0_attn_a_in['Wk'], 'L0_attn_a_bk': _L0_attn_a_in['bk'], 'L0_attn_a_Wv': _L0_attn_a_in['Wv'], 'L0_attn_a_bv': _L0_attn_a_in['bv'], 'L0_attn_a_Wo': _L0_attn_a_in['Wo'], 'L0_attn_a_bo': _L0_attn_a_in['bo'], 'L0_attn_a_rw': _L0_attn_a_in['rw'], 'L0_attn_b_Wq': _L0_attn_b_in['Wq'], 'L0_attn_b_bq': _L0_attn_b_in['bq'], 'L0_attn_b_Wk': _L0_attn_b_in['Wk'], 'L0_attn_b_bk': _L0_attn_b_in['bk'], 'L0_attn_b_Wv': _L0_attn_b_in['Wv'], 'L0_attn_b_bv': _L0_attn_b_in['bv'], 'L0_attn_b_Wo': _L0_attn_b_in['Wo'], 'L0_attn_b_bo': _L0_attn_b_in['bo'], 'L0_ffn_wqkv': _L0_ffn_in['wqkv'], 'L0_ffn_q_scale': _L0_ffn_in['q_scale'], 'L0_ffn_k_scale': _L0_ffn_in['k_scale'], 'L0_ffn_wo': _L0_ffn_in['wo'], 'L0_ffn_ln_g': _L0_ffn_in['ln_g'], 'L0_ffn_ln_b': _L0_ffn_in['ln_b'], 'L0_ffn_w1': _L0_ffn_in['w1'], 'L0_ffn_b1': _L0_ffn_in['b1'], 'L0_ffn_w2': _L0_ffn_in['w2'], 'L0_ffn_b2': _L0_ffn_in['b2']}
    _x0 = _d['L0_attn_a_x']
    _d['L0_attn_a_x'] = jax.random.normal(jax.random.fold_in(jax.random.key(seed), 1), (16, 256, 128), dtype=_x0.dtype)
    del _x0
    return _d

def reference(L0_attn_a_x, L0_attn_a_Wq, L0_attn_a_bq, L0_attn_a_Wk, L0_attn_a_bk, L0_attn_a_Wv, L0_attn_a_bv, L0_attn_a_Wo, L0_attn_a_bo, L0_attn_a_rw, L0_attn_b_Wq, L0_attn_b_bq, L0_attn_b_Wk, L0_attn_b_bk, L0_attn_b_Wv, L0_attn_b_bv, L0_attn_b_Wo, L0_attn_b_bo, L0_ffn_wqkv, L0_ffn_q_scale, L0_ffn_k_scale, L0_ffn_wo, L0_ffn_ln_g, L0_ffn_ln_b, L0_ffn_w1, L0_ffn_b1, L0_ffn_w2, L0_ffn_b2):

    def _L0_attn_a_ref(x, Wq, bq, Wk, bk, Wv, bv, Wo, bo, rw):
        import jax, jax.numpy as jnp
        import numpy as np
        B, S, D, H, F = (4, 1024, 128, 16, 64)
        DK = D // H
        EPS = 1e-06

        def _heads(x, W, b):
            y = jnp.einsum('bsd,de->bse', x, W) + b
            return y.reshape(x.shape[0], x.shape[1], H, DK).transpose(0, 2, 1, 3)
        q = _heads(x, Wq, bq)
        k = _heads(x, Wk, bk)
        v = _heads(x, Wv, bv)
        qp = jax.nn.relu(jnp.einsum('bhsd,hdf->bhsf', q, rw)) + EPS
        kp = jax.nn.relu(jnp.einsum('bhsd,hdf->bhsf', k, rw)) + EPS
        kv = jnp.einsum('bhsf,bhsd->bhfd', kp, v)
        qkv = jnp.einsum('bhsf,bhfd->bhsd', qp, kv)
        norm = jnp.einsum('bhsf,bhf->bhs', qp, kp.sum(axis=2))
        out = qkv / (norm[..., None] + EPS)
        out = out.transpose(0, 2, 1, 3).reshape(x.shape[0], x.shape[1], D)
        return jnp.einsum('bsd,de->bse', out, Wo) + bo

    def _L0_attn_b_ref(X_embed, Wq, bq, Wk, bk, Wv, bv, Wo, bo):
        import jax, jax.numpy as jnp
        import numpy as np
        HEADS = 16
        HIDDEN = 128
        N, L, _ = X_embed.shape
        H, heads = (HIDDEN, HEADS)
        dh = H // heads
        Q = X_embed @ Wq + bq
        K = X_embed @ Wk + bk
        V = X_embed @ Wv + bv
        Q = Q.reshape(N, heads, L, dh)
        K = K.reshape(N, heads, L, dh)
        V = V.reshape(N, heads, L, dh)
        scale = np.float32(1.0 / np.sqrt(H))
        Q = Q * scale
        K = K * scale
        scores = jnp.einsum('neax,nebx->neab', Q, K)
        A = jax.nn.softmax(scores, axis=2)
        Out = jnp.einsum('neab,neax->neax', A, V)
        Out = Out.reshape(N, L, H)
        return Out @ Wo + bo

    def _L0_ffn_ref(x, wqkv, q_scale, k_scale, wo, ln_g, ln_b, w1, b1, w2, b2):
        import jax, jax.numpy as jnp
        import numpy as np
        DIM = 128
        DEPTH = 2
        HEADS = 8
        DIM_HEAD = 64
        WINDOW = 64
        INNER = HEADS * DIM_HEAD
        HID = int(DIM * 4 * 2 / 3)
        B, N = (2, 1024)
        QK_SCALE = 8.0

        def shift_token(t):
            t1, t2 = jnp.split(t, 2, axis=-1)
            t2 = jnp.pad(t2, ((0, 0), (1, 0), (0, 0)))[:, :-1]
            return jnp.concatenate([t1, t2], axis=-1)

        def l2norm(t):
            return t / jnp.clip(jnp.linalg.norm(t, axis=-1, keepdims=True), 1e-12)

        def rotate_half(x):
            x1, x2 = jnp.split(x, 2, axis=-1)
            return jnp.concatenate([-x2, x1], axis=-1)

        def rotary_xpos(q, k):
            n = q.shape[-2]
            half_idx = jnp.arange(0, DIM_HEAD, 2, dtype=jnp.float32)
            inv_freq = 1.0 / 10000.0 ** (half_idx / DIM_HEAD)
            t = jnp.arange(n, dtype=jnp.float32)
            freqs = t[:, None] * inv_freq[None, :]
            freqs = jnp.concatenate([freqs, freqs], axis=-1)
            base = (half_idx + 0.4 * DIM_HEAD) / (1.4 * DIM_HEAD)
            power = (t - n // 2) / float(WINDOW // 2)
            scale = base[None, :] ** power[:, None]
            scale = jnp.concatenate([scale, scale], axis=-1)
            cos, sin = (jnp.cos(freqs), jnp.sin(freqs))
            q = q * cos * scale + rotate_half(q) * sin * scale
            k = k * cos / scale + rotate_half(k) * sin / scale
            return (q, k)

        def local_attention(q, k, v):
            b, h, n, d = q.shape
            w = n // WINDOW
            bq = q.reshape(b, h, w, WINDOW, d) * QK_SCALE
            bk = k.reshape(b, h, w, WINDOW, d)
            bv = v.reshape(b, h, w, WINDOW, d)

            def look_around(t):
                p = jnp.pad(t, ((0, 0), (0, 0), (1, 0), (0, 0), (0, 0)))
                return jnp.concatenate([p[:, :, :w], p[:, :, 1:]], axis=3)
            bk, bv = (look_around(bk), look_around(bv))
            bt = jnp.arange(n).reshape(w, WINDOW)
            btp = jnp.pad(bt, ((1, 0), (0, 0)), constant_values=-1)
            btk = jnp.concatenate([btp[:w], btp[1:]], axis=1)
            sim = jnp.einsum('bhwid,bhwjd->bhwij', bq, bk)
            i = bt[:, :, None]
            j = btk[:, None, :]
            mask = (i < j) | (i > j + WINDOW) | (j == -1)
            sim = jnp.where(mask, -jnp.finfo(sim.dtype).max, sim)
            attn = jax.nn.softmax(sim, axis=-1)
            out = jnp.einsum('bhwij,bhwjd->bhwid', attn, bv)
            return out.reshape(b, h, n, d)

        def _layer(x, wqkv, qs, ksc, wo, lg, lb, w1, b1, w2, b2):
            b, n, _ = x.shape
            h = shift_token(x)
            qkv = h @ wqkv
            q, k, v = jnp.split(qkv, 3, axis=-1)
            to_heads = lambda t: t.reshape(b, n, HEADS, DIM_HEAD).transpose(0, 2, 1, 3)
            q, k, v = (to_heads(q), to_heads(k), to_heads(v))
            q = l2norm(q) * qs
            k = l2norm(k) * ksc
            q, k = rotary_xpos(q, k)
            o = local_attention(q, k, v)
            o = o.transpose(0, 2, 1, 3).reshape(b, n, INNER)
            x = x + o @ wo
            h = shift_token(x)
            mu = h.mean(-1, keepdims=True)
            var = h.var(-1, keepdims=True)
            h = (h - mu) / jnp.sqrt(var + 1e-05) * lg + lb
            h = h @ w1 + b1
            a, g = jnp.split(h, 2, axis=-1)
            h = a * jax.nn.gelu(g, approximate=False)
            x = x + h @ w2 + b2
            return x
        for l in range(DEPTH):
            x = _layer(x, wqkv[l], q_scale[l], k_scale[l], wo[l], ln_g[l], ln_b[l], w1[l], b1[l], w2[l], b2[l])
        return x
    x = L0_attn_a_x
    x = x + _L0_attn_a_ref(_layernorm(x, axis=-1), L0_attn_a_Wq, L0_attn_a_bq, L0_attn_a_Wk, L0_attn_a_bk, L0_attn_a_Wv, L0_attn_a_bv, L0_attn_a_Wo, L0_attn_a_bo, L0_attn_a_rw)
    x = x + _L0_ffn_ref(_layernorm(x, axis=-1), L0_ffn_wqkv, L0_ffn_q_scale, L0_ffn_k_scale, L0_ffn_wo, L0_ffn_ln_g, L0_ffn_ln_b, L0_ffn_w1, L0_ffn_b1, L0_ffn_w2, L0_ffn_b2)
    x = x + _L0_attn_b_ref(_layernorm(x, axis=-1), L0_attn_b_Wq, L0_attn_b_bq, L0_attn_b_Wk, L0_attn_b_bk, L0_attn_b_Wv, L0_attn_b_bv, L0_attn_b_Wo, L0_attn_b_bo)
    x = x + _L0_ffn_ref(_layernorm(x, axis=-1), L0_ffn_wqkv, L0_ffn_q_scale, L0_ffn_k_scale, L0_ffn_wo, L0_ffn_ln_g, L0_ffn_ln_b, L0_ffn_w1, L0_ffn_b1, L0_ffn_w2, L0_ffn_b2)
    return x

_drawn_inputs = setup_inputs


def setup_inputs(seed=0):
    import zlib

    import numpy as np

    out = dict(_drawn_inputs(seed))
    spreads = {'L0_attn_a_bq': (0.0, 0.8),
     'L0_attn_a_bk': (0.0, 0.8),
     'L0_attn_a_bv': (0.0, 0.1),
     'L0_attn_a_bo': (0.0, 0.1),
     'L0_ffn_q_scale': (1.0, 0.6),
     'L0_ffn_k_scale': (1.0, 0.6),
     'L0_ffn_ln_g': (1.0, 0.6),
     'L0_ffn_ln_b': (0.0, 0.8),
     'L0_ffn_b1': (0.0, 0.8),
     'L0_ffn_b2': (0.0, 0.1)}
    factors = {'L0_attn_b_Wq': 64.0,
     'L0_attn_b_bq': 64.0,
     'L0_attn_b_Wk': 64.0,
     'L0_attn_b_bk': 64.0,
     'L0_attn_b_bv': 46.57,
     'L0_attn_b_bo': 5.474,
     'L0_ffn_w1': 3.755,
     'L0_ffn_w2': 3.725,
     'L0_attn_b_Wv': 4.88,
     'L0_attn_b_Wo': 4.154}
    for name, (base, spread) in spreads.items():
        noise = np.random.default_rng([zlib.crc32(name.encode()), seed]).standard_normal(out[name].shape)
        drawn = base * np.exp(spread * noise) if base else spread * noise
        out[name] = jnp.asarray(drawn.astype(out[name].dtype))
    for name, factor in factors.items():
        out[name] = (out[name] * factor).astype(out[name].dtype)
    return out
```

```python
from contextlib import ExitStack

import numpy as np

import concourse.bass as bass
from concourse import mybir

F32 = mybir.dt.float32
F32R = mybir.dt.float32r
BF16 = mybir.dt.bfloat16
ACT = mybir.ActivationFunctionType
ALU = mybir.AluOpType
AX = mybir.AxisListType

P = 128
SEQS, SEQ, DIM = 16, 256, 128
TOK = SEQS * SEQ
PAIR = 2 * SEQ
PAIRS = TOK // PAIR
DEPTH = 2
HEADS, DH, WINDOW = 8, 64, 64
INNER = HEADS * DH
CHUNKS = INNER // P
HID = int(DIM * 4 * 2 / 3)
HID_CHUNKS = [(0, P), (P, P), (2 * P, HID - 2 * P)]
EPS_LN = 1e-5
MASKED = -1e30
SS_SCALE = 2.0 ** 40
SS_BIAS = 2.0 ** -64


def rotary_tables():
    half = np.arange(0, DH, 2, dtype=np.float64)
    freq = 1.0 / 10000.0 ** (half / DH)
    t = np.arange(SEQ, dtype=np.float64)
    ang = t[:, None] * freq[None]
    base = (half + 0.4 * DH) / (1.4 * DH)
    scale = base[None] ** ((t - SEQ // 2) / (WINDOW // 2))[:, None]
    two = lambda a: np.concatenate([a, a], 1).T
    cos, sin, scale = two(np.cos(ang)), two(np.sin(ang)), two(scale)
    sign = np.where(np.arange(DH) < DH // 2, -1.0, 1.0)[:, None]
    qk_scale = 8.0
    tabs = [cos * scale * qk_scale, sign * sin * scale * qk_scale, cos / scale, sign * sin / scale]
    return np.stack([np.concatenate([a, a], 0) for a in tabs]).astype(np.float32)


def window_masks():
    i = np.arange(P)[:, None]
    m0 = i - np.arange(P)[None]
    m1 = (P + i) - (WINDOW + np.arange(3 * WINDOW)[None])
    return np.concatenate([np.where((d >= 0) & (d <= WINDOW), 0.0, MASKED) for d in (m0, m1)], 1)


def constants():
    return {
        "c_rot": rotary_tables(),
        "c_mask": window_masks().astype(np.float32),
        "c_ident": np.eye(P, dtype=np.float32),
        "c_mean": np.full((P, P), 1.0 / DIM, np.float32),
        "c_head": np.kron(np.eye(2), np.ones((DH, DH))).astype(np.float32),
    }


def load_block(nc, K):
    with nc.Block() as block:
        @block.sync
        def _(sp):
            sp.dma_start(K.ident[:], K.d["c_ident"]).then_inc(K.s.const_in, 16)
            sp.dma_start(K.tok[:], K.d["L0_attn_a_x"].rearrange("b (u p) c -> p (b u) c", p=P)).then_inc(K.s.x_in, 16)
            sp.dma_start(K.rot[:], K.d["c_rot"].rearrange("k p t -> p k t")).then_inc(K.s.const_in, 16)
            sp.dma_start(K.rsum[:, 0, 0, 0:P + 192], K.d["c_mask"]).then_inc(K.s.const_in, 16)
            sp.dma_start(K.mean_w[:], K.d["c_mean"]).then_inc(K.s.const_in, 16)
            sp.dma_start(K.head_w[:], K.d["c_head"]).then_inc(K.s.const_in, 16)
            sp.wait_ge(K.s.const_in, 16 * 5)

        @block.gpsimd
        def _(pool):
            for semaphore in K.s.primed:
                pool.sem_inc(semaphore, 1)
            pool.memset(K.eps[:], EPS_LN)
            pool.memset(K.ssb[:], SS_BIAS)
            pool.memset(K.rsb[:], float(20.0 * np.log(2.0)))

        @block.tensor
        def _(pe):
            pe.wait_ge(K.s.const_in, 16 * 5)
            pe.wait_ge(K.s.x_in, 16)
            for j in range(PAIRS):
                if j >= 2:
                    pe.wait_ge(K.s.xt_out, j - 1)
                for q in range(4):
                    mm = pe.transpose(K.proj[j % 2][:, q * P:(q + 1) * P], K.tok[:, 4 * j + q, :], K.ident[:])
                mm.then_inc(K.s.xt_done, 1)

        @block.vector
        def _(dve):
            dve.wait_ge(K.s.const_in, 16 * 5)
            dve.tensor_copy(K.mask[:], K.rsum[:, 0, 0, 0:P + 192])
            dve.tensor_copy(K.identb[:], K.ident[:])
            for j in range(PAIRS):
                dve.wait_ge(K.s.xt_done, j + 1)
                dve.tensor_copy(K.X[:, j * PAIR:(j + 1) * PAIR], K.proj[j % 2][:]).then_inc(K.s.xt_out, 1)


def store_block(nc, K):
    with nc.Block() as block:
        @block.vector
        def _(dve):
            for j in range(PAIRS):
                sl = slice(j * PAIR, (j + 1) * PAIR)
                dve.tensor_tensor(K.X[:, sl], K.X[:, sl], K.Y[:, sl], ALU.add).then_inc(K.s.fin_sum, 1)
            for j in range(PAIRS):
                dve.wait_ge(K.s.fin_t, j + 1)
                dve.tensor_copy(K.tok[:, 4 * j:4 * j + 4, :], K.proj[j % 2][:].rearrange("p (q c) -> p q c", c=P)).then_inc(K.s.fin_out, 1)

        @block.tensor
        def _(pe):
            for j in range(PAIRS):
                pe.wait_ge(K.s.fin_sum, j + 1)
                if j >= 2:
                    pe.wait_ge(K.s.fin_out, j - 1)
                for q in range(4):
                    t0 = j * PAIR + q * P
                    mm = pe.transpose(K.proj[j % 2][:, q * P:(q + 1) * P], K.X[:, t0:t0 + P], K.ident[:])
                mm.then_inc(K.s.fin_t, 1)

        @block.sync
        def _(sp):
            out = K.out.rearrange("b (u p) c -> p (b u) c", p=P)
            for j in range(PAIRS):
                sp.wait_ge(K.s.fin_out, j + 1)
                sp.dma_start(out[:, 4 * j:4 * j + 4, :], K.tok[:, 4 * j:4 * j + 4, :]).then_inc(K.s.stored, 16)
            sp.wait_ge(K.s.stored, 16 * PAIRS)


def norm_block(nc, K, n, add_y=False, shift=False, affine=False, split=False):
    S = K.s
    HALF_RUN = PAIRS // 2
    src = K.Y if shift else K.X
    if shift:
        with nc.Block() as block:
            @block.gpsimd
            def _(pool):
                pool.memset(K.lns[:], 0.0)

    with nc.Block() as block:
        @block.gpsimd
        def _(pool):

            with pool.Fori(0, HALF_RUN) as i:
                g = n * HALF_RUN + i
                for b in range(2):
                    t0 = (i * 2 + b) * PAIR
                    if shift:
                        if b == 0:
                            pool.wait_ge(S.ln_cent, 1 + 2 * g)
                        pool.tensor_copy(K.lns[0:64, b], src[0:64, bass.ds(t0, PAIR)])
                        a = src[64:128, bass.ds(t0, PAIR)].rearrange("p (s t) -> p s t", s=2)
                        o = K.lns[64:128, b].rearrange("p (s t) -> p s t", s=2)
                        pool.tensor_copy(o[:, :, 1:SEQ], a[:, :, 0:SEQ - 1]).then_inc(S.ln_src, 1)
                    elif add_y:
                        if b == 0:
                            pool.wait_ge(S.ln_cent, 1 + 2 * g)
                        pool.tensor_tensor(K.lns[:, b], K.X[:, bass.ds(t0, PAIR)], K.Y[:, bass.ds(t0, PAIR)], ALU.add).then_inc(S.ln_src, 1)
                    else:
                        if b == 0:
                            pool.wait_ge(S.ln_cent, 1 + 2 * g)
                        pool.tensor_copy(K.lns[:, b], K.X[:, bass.ds(t0, PAIR)]).then_inc(S.ln_src, 1)

        @block.tensor
        def _(pe):
            with pe.Fori(0, HALF_RUN) as i:
                g = n * HALF_RUN + i
                for b in range(2):
                    pe.wait_ge(S.ln_src, 2 * g + b + 1)
                    pe.wait_ge(S.ln_cent, 1 + 2 * g + b)
                    pe.matmul(K.proj[b][:], K.mean_w[:], K.lns[:, b], start=True, stop=True).then_inc(S.ln_mean, 1)
                for b in range(2):
                    pe.wait_ge(S.ln_sq, 2 * g + b + 1)
                    pe.matmul(K.sc[b][:], K.mean_w[:], K.lnq[:, b], start=True, stop=True).then_inc(S.ln_var, 1)

        @block.scalar
        def _(act):
            act.preload_act_table_set("natural_log_exp_and_others")
            with act.Fori(0, HALF_RUN) as i:
                g = n * HALF_RUN + i
                for b in range(2):
                    act.wait_ge(S.ln_cent, 1 + 2 * g + b + 1)
                    act.activation(K.lnq[:, b], K.lnd[:, b], ACT.Square).then_inc(S.ln_sq, 1)
                for b in range(2):
                    act.wait_ge(S.ln_var, 2 * g + b + 1)
                    act.activation(K.lnl[:, b], K.sc[b][:], ACT.Ln, bias=K.eps[:]).then_inc(S.ln_log, 1)
                    act.wait_ge(S.ln_log, 2 * g + b + 1)
                    act.activation(K.lnr[:, b], K.lnl[:, b], ACT.Exp, scale=-0.5).then_inc(S.ln_rstd, 1)

        @block.vector
        def _(dve):
            with dve.Fori(0, HALF_RUN) as i:
                g = n * HALF_RUN + i
                for b in range(2):
                    t0 = (i * 2 + b) * PAIR
                    dve.wait_ge(S.ln_mean, 2 * g + b + 1)
                    if add_y:
                        dve.tensor_copy(K.X[:, bass.ds(t0, PAIR)], K.lns[:, b])
                    dve.wait_ge(S.ln_nrm, 1 + 2 * g)
                    dve.tensor_tensor(K.lnd[:, b], K.lns[:, b], K.proj[b][:], ALU.subtract).then_inc(S.ln_cent, 1)
                for b in range(2):
                    t0 = (i * 2 + b) * PAIR
                    sl = bass.ds(t0, PAIR)
                    dve.wait_ge(S.ln_rstd, 2 * g + b + 1)
                    out = K.lnf[:, b] if (split or affine) else K.Y[:, sl]
                    dve.tensor_tensor(out, K.lnd[:, b], K.lnr[:, b], ALU.mult).then_inc(S.ln_nrm, 1)
                    if affine:
                        dve.wait_ge(S.ln_nrm, 1 + 2 * g + b + 1)
                        dve.tensor_scalar(K.lng[:, b], K.lnf[:, b], K.colp[:, 0:1], K.colp[:, 1:2], ALU.mult, ALU.add).then_inc(S.ln_aff, 1)
                for b in range(2):
                    if split:
                        t0 = (i * 2 + b) * PAIR
                        sl = bass.ds(t0, PAIR)
                        val = K.lng if affine else K.lnf
                        if affine:
                            dve.wait_ge(S.ln_aff, 2 * (K.aff_n * HALF_RUN + i) + b + 1)
                        else:
                            dve.wait_ge(S.ln_nrm, 1 + 2 * g + b + 1)
                        dve.tensor_copy(K.HI[:, sl], val[:, b]).then_inc(S.ln_hi, 1)
                        dve.wait_ge(S.ln_hi, 2 * (K.split_n * HALF_RUN + i) + b + 1)
                        dve.tensor_tensor(K.LO[:, sl], val[:, b], K.HI[:, sl].bitcast(F32), ALU.subtract)


def weights_block(nc, K, l, n):
    S = K.s
    d = K.d
    L = bass.ds(l, 1)
    n_dma = 0
    with nc.Block() as block:
        @block.sync
        def _(sp):
            loads = [
                (K.stage[:, 0:3 * INNER], d["L0_ffn_wqkv"][L].rearrange("a p n -> p (a n)")),
                (K.wo[:], d["L0_ffn_wo"][L].rearrange("a (c p) n -> p (a c) n", p=P)),
                (K.stage1[:], d["L0_ffn_w1"][L].rearrange("a p n -> p (a n)")),
                (K.w2[:, 0:2, :], d["L0_ffn_w2"][L, 0:2 * P].rearrange("a (c p) n -> p (a c) n", p=P)),
                (K.w2[0:HID - 2 * P, 2, :], d["L0_ffn_w2"][L, 2 * P:HID].rearrange("a p n -> p (a n)")),
                (K.colp[:, 0:1], d["L0_ffn_ln_g"][L].rearrange("a (p o) -> p (a o)", o=1)),
                (K.colp[:, 1:2], d["L0_ffn_ln_b"][L].rearrange("a (p o) -> p (a o)", o=1)),
                (K.colp[:, 2:3], d["L0_ffn_b2"][L].rearrange("a (p o) -> p (a o)", o=1)),
            ]
            for m, (h0, hn) in enumerate(HID_CHUNKS):
                for side in range(2):
                    loads.append((K.colb[0:hn, 2 * m + side:2 * m + side + 1],
                                  d["L0_ffn_b1"][L, side * HID + h0:side * HID + h0 + hn].rearrange("a (p o) -> p (a o)", o=1)))
            for k, name in enumerate(("L0_ffn_q_scale", "L0_ffn_k_scale")):
                for e in range(2):
                    loads.append((K.cols[e * DH:(e + 1) * DH, 2 * k:2 * k + 1], d[name][L].rearrange("a (p o) -> p (a o)", o=1)))
                    for h in range(2):
                        lo = e * DH + h * 32
                        loads.append((K.cols[lo:lo + 32, 2 * k + 1:2 * k + 2],
                                      d[name][L, (1 - h) * 32:(2 - h) * 32].rearrange("a (p o) -> p (a o)", o=1)))
            for dst, src in loads:
                sp.dma_start(dst, src).then_inc(S.w_in, 16)

            K.n_loads = len(loads)

        @block.vector
        def _(dve):
            dve.wait_ge(S.w_in, (n + 1) * 16 * K.n_loads)
            for k in range(2):
                w = K.stage[:, k * INNER:(k + 1) * INNER]
                dve.tensor_copy(K.wqk_hi[:, 2 * k], w).then_inc(S.w_hi, 1)
                wv = w.rearrange("p (h a d) -> p h a d", a=2, d=32)
                sw = K.wqk_hi[:, 2 * k + 1].rearrange("p (h a d) -> p h a d", a=2, d=32)
                for a in range(2):
                    dve.tensor_copy(sw[:, :, a], wv[:, :, 1 - a]).then_inc(S.w_hi, 1)
            dve.tensor_copy(K.wv_hi[:], K.stage[:, 2 * INNER:3 * INNER]).then_inc(S.w_hi, 1)
            dve.tensor_copy(K.w1_hi[:], K.stage1[:]).then_inc(S.w_hi, 1)
            for k in range(4):
                dve.tensor_scalar(K.tab[:, k], K.rot[:, k], K.cols[:, k:k + 1], None, ALU.mult)
            dve.wait_ge(S.w_hi, 8 * n + 8)
            for k in range(2):
                w = K.stage[:, k * INNER:(k + 1) * INNER]
                dve.tensor_tensor(K.wqk_lo[:, 2 * k], w, K.wqk_hi[:, 2 * k].bitcast(F32), ALU.subtract)
                wv = w.rearrange("p (h a d) -> p h a d", a=2, d=32)
                sw = K.wqk_hi[:, 2 * k + 1].rearrange("p (h a d) -> p h a d", a=2, d=32)
                sl = K.wqk_lo[:, 2 * k + 1].rearrange("p (h a d) -> p h a d", a=2, d=32)
                for a in range(2):
                    dve.tensor_tensor(sl[:, :, a], wv[:, :, 1 - a], sw[:, :, a].bitcast(F32), ALU.subtract)
            dve.tensor_tensor(K.wv_lo[:], K.stage[:, 2 * INNER:3 * INNER], K.wv_hi[:].bitcast(F32), ALU.subtract)
            dve.tensor_tensor(K.w1_lo[:], K.stage1[:], K.w1_hi[:].bitcast(F32), ALU.subtract)


UNITS = 3
EXPS_AFTER = (4, 6, 8)


def attention_block(nc, K, n):
    S = K.s
    NPROJ = 4 + 4 * CHUNKS

    def prods(x):
        return x.rearrange("p (s t) -> p s t", s=2)

    with nc.Block() as block:
        @block.tensor
        def _(pe):
            with pe.Fori(0, PAIRS) as p:
                g = n * PAIRS + p

                def split_product(bank, lhs, rhs):
                    pe.matmul(bank, lhs[0], rhs[0], start=True, stop=False)
                    pe.matmul(bank, lhs[0], rhs[1], start=False, stop=False)
                    return pe.matmul(bank, lhs[1], rhs[0], start=False, stop=True)

                pe.wait_ge(S.h_lo, 2 * (g + 1))
                for t in range(4):
                    if t < 2:
                        pe.wait_ge(S.prod, 1 + 16 * g)
                    else:
                        pe.wait_ge(S.v_out, 4 * g + t - 1)
                    sl = slice(t * P, (t + 1) * P)
                    split_product(K.proj[t % 2][:], (K.hhi[:, sl], K.hlo[:, sl]), (K.wv_hi[:], K.wv_lo[:])).then_inc(S.proj, 1)

                for k in range(CHUNKS + 2):
                    if k < CHUNKS:
                        for j in range(4):
                            if k == 0 and j < 2:
                                pe.wait_ge(S.v_out, 4 * g + 3 + j)
                            else:
                                pe.wait_ge(S.prod, 1 + 16 * g + 4 * k + j - 1)
                            sl = slice(k * P, (k + 1) * P)
                            split_product(K.proj[j % 2][:], (K.wqk_hi[:, j, sl], K.wqk_lo[:, j, sl]),
                                          (K.hhi[:], K.hlo[:])).then_inc(S.proj, 1)
                    if 1 <= k <= CHUNKS:
                        c = k - 1
                        b = c % 2
                        pe.wait_ge(S.k_rot, 8 * g + 2 * c + 2)
                        for u in range(UNITS):
                            x = UNITS * c + u
                            if x >= 2:
                                pe.wait_ge(S.ex, 32 * g + 8 * ((x - 2) // 3) + EXPS_AFTER[(x - 2) % 3])
                            bank = K.sc[x % 2]
                            if u == 0:
                                pe.matmul(bank[:].rearrange("p (a j) -> p a j", a=4), K.identb[:],
                                          K.mask[:, 0:P].unsqueeze(1).broadcast_to([P, 4, P]), start=True, stop=False)
                                for s in range(2):
                                    mm = pe.matmul(bank[:, s * 256:(s + 1) * 256].rearrange("p (e j) -> p e j", e=2),
                                                   K.qrot[:, b, s * SEQ:s * SEQ + P],
                                                   K.kpad[:, b, :, s * SEQ:s * SEQ + P], start=False, stop=(s == 1))
                            else:
                                s = u - 1
                                out = bank[:, 0:384].rearrange("p (e j) -> p e j", e=2)
                                pe.matmul(out, K.identb[:], K.mask[:, P:P + 192].unsqueeze(1).broadcast_to([P, 2, 192]),
                                          start=True, stop=False)
                                mm = pe.matmul(out, K.qrot[:, b, s * SEQ + P:(s + 1) * SEQ],
                                               K.kpad[:, b, :, s * SEQ + WINDOW:(s + 1) * SEQ], start=False, stop=True)
                            mm.then_inc(S.scores, 1)
                    if k < CHUNKS:
                        for j in range(2):
                            pe.wait_ge(S.sq, 8 * g + 2 * k + j + 1)
                            pe.wait_ge(S.ln_ss, 1 + 8 * g + 2 * k + j)
                            pe.matmul(K.ss[:], K.head_w[:], K.sqb[:, j], start=True, stop=True).then_inc(S.ss, 1)
                    if k >= 3:
                        c = k - 3
                        pe.wait_ge(S.pt_act, 1 + 8 * g + 2 * c + 1)
                        pe.wait_ge(S.onorm, 4 * g + c + 1)
                        for t in range(4):
                            mm = pe.transpose(K.pt[1][:, t * P:(t + 1) * P], K.on[:, c % 2, t], K.ident[:])
                        mm.then_inc(S.ptd, 1)
                    if k >= 2:
                        c = k - 2
                        b = c % 2
                        for u in range(UNITS):
                            pe.wait_ge(S.ex, 32 * g + 8 * c + EXPS_AFTER[u])
                            if u == 1:
                                pe.wait_ge(S.pt_act, 1 + 8 * g + 2 * c)
                            else:
                                pe.wait_ge(S.pt_dve, 1 + 8 * g + 2 * c + u // 2)
                            for a in range(4):
                                if u == 0:
                                    blk = K.p0[:, b, a]
                                else:
                                    blk = K.p1[:, b, 2 * (u - 1) + a // 2, (a % 2) * P:(a % 2 + 1) * P]
                                mm = pe.transpose(K.pt[u % 2][:, a * P:(a + 1) * P], blk, K.ident[:])
                            mm.then_inc(S.ptd, 1)
                        if c == 0:
                            pe.wait_ge(S.y_upd, 1 + g)
                        else:
                            pe.wait_ge(S.onorm, 4 * g + c)
                        pe.wait_ge(S.pt_dve, 1 + 8 * g + 2 * c + 2)
                        pe.wait_ge(S.pt_act, 1 + 8 * g + 2 * c + 1)
                        for s in range(2):
                            for e in range(2):
                                hc = slice((2 * c + e) * DH, (2 * c + e + 1) * DH)
                                o0 = (2 * s) * P + e * DH
                                pe.matmul(K.ob[:, o0:o0 + DH], K.ptb[:, b, 0, 2 * s + e], K.v[:, 2 * s, hc], start=True, stop=True)
                                o1 = (2 * s + 1) * P + e * DH
                                pe.matmul(K.ob[:, o1:o1 + DH], K.ptb[:, b, 1 + s, 2 * e], K.v[:, 2 * s, hc], start=True, stop=False)
                                mm = pe.matmul(K.ob[:, o1:o1 + DH], K.ptb[:, b, 1 + s, 2 * e + 1], K.v[:, 2 * s + 1, hc],
                                               start=False, stop=True)
                        mm.then_inc(S.pv, 1)
                c = CHUNKS - 1
                pe.wait_ge(S.pt_act, 1 + 8 * g + 2 * c + 1)
                pe.wait_ge(S.onorm, 4 * g + c + 1)
                for t in range(4):
                    mm = pe.transpose(K.pt[1][:, t * P:(t + 1) * P], K.on[:, c % 2, t], K.ident[:])
                mm.then_inc(S.ptd, 1)
                pe.wait_ge(S.pt_act, 1 + 8 * g + 8)
                for c in range(CHUNKS):
                    mm = pe.matmul(K.ob[:], K.wo[:, c], K.ot[:, c], start=(c == 0), stop=(c == CHUNKS - 1))
                mm.then_inc(S.wo, 1)

        @block.scalar
        def _(act):
            act.preload_act_table_set("natural_log_exp_and_others")
            with act.Fori(0, PAIRS) as p:
                g = n * PAIRS + p
                for t in range(4):
                    act.wait_ge(S.proj, 1 + NPROJ * g + t + 1)
                    act.copy(K.v[:, t], K.proj[t % 2][:]).then_inc(S.v_out, 1)
                for k in range(CHUNKS + 2):
                    if k < CHUNKS:
                        for j in range(2):
                            act.wait_ge(S.proj, 1 + NPROJ * g + 4 + 4 * k + 2 * j + 1)
                            act.activation(K.sqb[:, j], K.proj[0][:], ACT.Square).then_inc(S.sq, 1)
                    if 1 <= k <= CHUNKS:
                        c = k - 1
                        b = c % 2
                        for u in range(UNITS):
                            act.wait_ge(S.mx, 12 * g + UNITS * c + u + 1)
                            bank = K.sc[(UNITS * c + u) % 2]
                            for a in range(4 if u == 0 else 2):
                                if u == 0:
                                    s, e, src, dst = a // 2, a % 2, bank[:, a * P:(a + 1) * P], K.p0[:, b, a]
                                    col = 4 * s + e
                                else:
                                    s, e, src = u - 1, a, bank[:, a * 192:(a + 1) * 192]
                                    dst = K.p1[:, b, 2 * s + e, WINDOW:SEQ]
                                    col = 4 * s + 2 + e
                                act.activation(dst, src, ACT.Exp, bias=K.nmax[:, b, col:col + 1],
                                               accum_out=K.den[:, b, col:col + 1]).then_inc(S.ex, 1)
                    if k < CHUNKS:
                        for j in range(2):
                            act.wait_ge(S.ss, 8 * g + 2 * k + j + 1)
                            act.activation(K.lss[:, j], K.ss[:], ACT.Ln, scale=SS_SCALE, bias=K.ssb[:]).then_inc(S.ln_ss, 1)
                            act.wait_ge(S.ln_ss, 1 + 8 * g + 2 * k + j + 1)
                            act.activation(K.rn[:, k % 2, j], K.lss[:, j], ACT.Exp, scale=-0.5, bias=K.rsb[:]).then_inc(S.rn, 1)
                    if k >= 3:
                        act.wait_ge(S.ptd, 16 * g + 4 * (k - 3) + 4)
                        act.copy(K.ot[:, k - 3], K.pt[1][:]).then_inc(S.pt_act, 1)
                    if k >= 2:
                        c = k - 2
                        act.wait_ge(S.ptd, 16 * g + 4 * c + 2)
                        act.copy(K.ptb[:, c % 2, 1], K.pt[1][:].rearrange("p (a i) -> p a i", a=4)).then_inc(S.pt_act, 1)
                act.wait_ge(S.ptd, 16 * g + 16)
                act.copy(K.ot[:, CHUNKS - 1], K.pt[1][:]).then_inc(S.pt_act, 1)

        @block.gpsimd
        def _(pool):
            with pool.Fori(0, PAIRS) as p:
                g = n * PAIRS + p
                for k in range(CHUNKS):
                    for j in range(2):
                        pool.wait_ge(S.prod, 1 + 16 * g + 4 * k + 2 * j + 2)
                        pool.tensor_tensor(K.rsum[:, k % 2, j], K.pa[:, k % 2, j], K.pb[:, k % 2, j], ALU.add).then_inc(S.rsum, 1)

        @block.vector
        def _(dve):
            with dve.Fori(0, PAIRS) as p:
                g = n * PAIRS + p
                t0 = p * PAIR
                ylo = K.Y[0:64, bass.ds(t0, PAIR)]
                yup = K.Y[64:128, bass.ds(t0, PAIR)].rearrange("p (s t) -> p s t", s=2)[:, :, 0:SEQ - 1]
                hhi_up = K.hhi[64:128].rearrange("p (s t) -> p s t", s=2)[:, :, 1:SEQ]
                hlo_up = K.hlo[64:128].rearrange("p (s t) -> p s t", s=2)[:, :, 1:SEQ]
                dve.wait_ge(S.proj, 1 + NPROJ * g)
                dve.tensor_copy(K.hhi[0:64], ylo).then_inc(S.h_hi, 1)
                dve.tensor_copy(hhi_up, yup).then_inc(S.h_hi, 1)
                dve.wait_ge(S.h_hi, 2 * (g + 1))
                dve.tensor_tensor(K.hlo[0:64], ylo, K.hhi[0:64].bitcast(F32), ALU.subtract).then_inc(S.h_lo, 1)
                dve.tensor_tensor(hlo_up, yup, hhi_up.bitcast(F32), ALU.subtract).then_inc(S.h_lo, 1)
                for k in range(CHUNKS + 2):
                    if k < CHUNKS:
                        b = k % 2
                        for j in range(4):
                            dst = (K.pa if j % 2 == 0 else K.pb)[:, b, j // 2]
                            tab = K.tab[:, j].unsqueeze(1).broadcast_to([P, 2, SEQ])
                            if j % 2 == 0:
                                dve.wait_ge(S.sq, 8 * g + 2 * k + j // 2 + 1)
                            else:
                                dve.wait_ge(S.proj, 1 + NPROJ * g + 4 + 4 * k + j + 1)
                            dve.tensor_tensor(prods(dst), prods(K.proj[j % 2][:]), tab, ALU.mult).then_inc(S.prod, 1)
                    if 1 <= k <= CHUNKS:
                        c = k - 1
                        for u in range(UNITS):
                            dve.wait_ge(S.scores, 12 * g + UNITS * c + u + 1)
                            bank = K.sc[(UNITS * c + u) % 2]
                            if u == 0:
                                src = bank[:].rearrange("p (s e j) -> p s e j", s=2, e=2)
                                dst = K.nmax[:, c % 2].rearrange("p (s u e) -> p s u e", u=2, e=2)[:, :, 0]
                            else:
                                src = bank[:, 0:384].rearrange("p (e j) -> p e j", e=2)
                                dst = K.nmax[:, c % 2, 4 * (u - 1) + 2:4 * (u - 1) + 4]
                            dve.tensor_reduce(dst, src, AX.X, ALU.max, negate=True).then_inc(S.mx, 1)
                    if k >= 2:
                        c = k - 2
                        b = c % 2
                        for u in (0, 2):
                            dve.wait_ge(S.ptd, 16 * g + 4 * c + u + 1)
                            dve.tensor_copy(K.ptb[:, b, u], K.pt[0][:].rearrange("p (a i) -> p a i", a=4)).then_inc(S.pt_dve, 1)
                        dve.wait_ge(S.ex, 32 * g + 8 * c + 8)
                        dve.reciprocal(K.rden[:, b], K.den[:, b]).then_inc(S.rden, 1)
                        dve.wait_ge(S.rden, 4 * g + c + 1)
                        dve.wait_ge(S.pv, 4 * g + c + 1)
                        dve.tensor_tensor(K.on[:, b].rearrange("p t (e d) -> p (t e) d", e=2),
                                          K.ob[:].rearrange("p (a d) -> p a d", d=DH),
                                          K.rden[:, b].unsqueeze(2).broadcast_to([P, 8, DH]), ALU.mult).then_inc(S.onorm, 1)
                    if k < CHUNKS:
                        b = k % 2
                        dve.wait_ge(S.rsum, 8 * g + 2 * k + 1)
                        dve.wait_ge(S.rn, 8 * g + 2 * k + 1)
                        dve.scalar_tensor_tensor(K.qrot[:, b], K.rn[:, b, 0], 1e12, K.rsum[:, b, 0], ALU.min, ALU.mult).then_inc(S.q_rot, 1)
                        dve.wait_ge(S.rsum, 8 * g + 2 * k + 2)
                        dve.wait_ge(S.rn, 8 * g + 2 * k + 2)
                        for e in range(2):
                            r = slice(e * DH, (e + 1) * DH)
                            dve.scalar_tensor_tensor(K.kpad[r, b, e], K.rn[r, b, 1], 1e12, K.rsum[r, b, 1],
                                                     ALU.min, ALU.mult).then_inc(S.k_rot, 1)
                dve.wait_ge(S.wo, g + 1)
                dve.tensor_tensor(K.Y[:, bass.ds(t0, PAIR)], K.ob[:], K.Y[:, bass.ds(t0, PAIR)], ALU.add).then_inc(S.y_upd, 1)


def geglu_block(nc, K, n):
    S = K.s
    NM = len(HID_CHUNKS)
    with nc.Block() as block:
        @block.tensor
        def _(pe):
            with pe.Fori(0, PAIRS // 2) as i:
                g = n * (PAIRS // 2) + i

                def down(b, m):
                    hn = HID_CHUNKS[m][1]
                    pe.wait_ge(S.u, 6 * g + 3 * b + m + 1)
                    if m == 0:
                        pe.wait_ge(S.ff_y, 1 + 2 * g + b)
                    mm = pe.matmul(K.ob[:], K.w2[0:hn, m], K.u[0:hn, (3 * b + m) % 2], start=(m == 0), stop=(m == NM - 1))
                    mm.then_inc(S.dn, 1)

                for b in range(2):
                    sl = bass.ds((i * 2 + b) * PAIR, PAIR)
                    for m, (h0, hn) in enumerate(HID_CHUNKS):
                        x = 3 * b + m
                        for side in (1, 0):
                            bank = (K.proj if side else K.sc)[x % 2]
                            if x >= 2:
                                pe.wait_ge(S.gl if side else S.u, 6 * g + x - 1)
                            lo = side * HID + h0
                            pe.matmul(bank[0:hn, :], K.w1_hi[:, lo:lo + hn], K.HI[:, sl], start=True, stop=False)
                            pe.matmul(bank[0:hn, :], K.w1_hi[:, lo:lo + hn], K.LO[:, sl], start=False, stop=False)
                            pe.matmul(bank[0:hn, :], K.w1_lo[:, lo:lo + hn], K.HI[:, sl], start=False, stop=True).then_inc(S.up, 1)
                        if x >= 1:
                            down((x - 1) // 3, (x - 1) % 3)
                down(1, NM - 1)

        @block.scalar
        def _(act):
            act.preload_act_table_set("gelu_and_others")
            with act.Fori(0, PAIRS // 2) as i:
                g = n * (PAIRS // 2) + i
                for x in range(6):
                    hn = HID_CHUNKS[x % 3][1]
                    m = x % 3
                    act.wait_ge(S.up, 12 * g + 2 * x + 1)
                    if x >= 2:
                        act.wait_ge(S.u, 6 * g + x - 1)
                    act.activation(K.gl[0:hn, x % 2], K.proj[x % 2][0:hn, :], ACT.Gelu,
                                   bias=K.colb[0:hn, 2 * m + 1:2 * m + 2]).then_inc(S.gl, 1)

        @block.vector
        def _(dve):
            with dve.Fori(0, PAIRS // 2) as i:
                g = n * (PAIRS // 2) + i

                def residual(b):
                    sl = bass.ds((i * 2 + b) * PAIR, PAIR)
                    dve.wait_ge(S.dn, 6 * g + 3 * b + 3)
                    dve.scalar_tensor_tensor(K.Y[:, sl], K.ob[:], K.colp[:, 2:3], K.Y[:, sl], ALU.add, ALU.add).then_inc(S.ff_y, 1)

                for x in range(6):
                    m = x % 3
                    hn = HID_CHUNKS[m][1]
                    dve.wait_ge(S.up, 12 * g + 2 * x + 2)
                    dve.wait_ge(S.gl, 6 * g + x + 1)
                    if x >= 2:
                        dve.wait_ge(S.dn, 6 * g + x - 1)
                    dve.scalar_tensor_tensor(K.u[0:hn, x % 2], K.sc[x % 2][0:hn, :], K.colb[0:hn, 2 * m:2 * m + 1],
                                             K.gl[0:hn, x % 2], ALU.add, ALU.mult).then_inc(S.u, 1)
                    if x == 3:
                        residual(0)
                residual(1)


A_HEADS, A_DK, A_F = 16, 8, 64
A_FEAT = A_HEADS * A_F
A_M = A_FEAT // P
A_EPS = 1e-6
A_OUT = 2 * A_DK + 2


def linear_attention_block(nc, K, A):
    S = K.s
    d = K.d
    names = ("Wq", "Wk", "Wv", "Wo")

    with nc.Block() as block:
        @block.gpsimd
        def _(pool):
            pool.memset(A.bd[:], 0.0).then_inc(S.a_zero, 1)
            pool.memset(A.kvbd[:], 0.0)
            pool.memset(A.v[:], 1.0)
            pool.memset(A.eps[:], A_EPS)

        @block.sync
        def _(sp):
            for k, name in enumerate(names):
                sp.dma_start(A.w[:, k], d["L0_attn_a_" + name]).then_inc(S.a_in, 16)
            for k, name in enumerate(("bq", "bk", "bo")):
                sp.dma_start(A.b[:, k:k + 1], d["L0_attn_a_" + name].rearrange("(p o) -> p o", o=1)).then_inc(S.a_in, 16)
            sp.dma_start(A.bv[:], d["L0_attn_a_bv"].partition_broadcast(P)).then_inc(S.a_in, 16)
            sp.wait_ge(S.a_zero, 1)
            for h in range(A_HEADS):
                sp.dma_start(A.bd[h * A_DK:(h + 1) * A_DK, h * A_F:(h + 1) * A_F], d["L0_attn_a_rw"][h]).then_inc(S.a_in, 16)

        @block.vector
        def _(dve):
            dve.wait_ge(S.a_in, 16 * (8 + A_HEADS))
            dve.tensor_copy(A.w_hi[:], A.w[:, 0:3]).then_inc(S.a_whi, 1)
            dve.tensor_copy(A.bd_hi[:], A.bd[:]).then_inc(S.a_whi, 1)
            dve.wait_ge(S.a_whi, 2)
            dve.tensor_tensor(A.w_lo[:], A.w[:, 0:3], A.w_hi[:].bitcast(F32), ALU.subtract)
            dve.tensor_tensor(A.bd_lo[:], A.bd[:], A.bd_hi[:].bitcast(F32), ALU.subtract)

    with nc.Block() as block:
        @block.tensor
        def _(pe):
            with pe.Fori(0, PAIRS) as g:
                sl = bass.ds(g * PAIR, PAIR)

                def split_product(bank, lhs, rhs):
                    pe.matmul(bank, lhs[0], rhs[0], start=True, stop=False)
                    pe.matmul(bank, lhs[0], rhs[1], start=False, stop=False)
                    return pe.matmul(bank, lhs[1], rhs[0], start=False, stop=True)

                pe.wait_ge(S.a_yc, g + 1)
                pe.wait_ge(S.a_qe, 1 + 8 * g)
                for j in range(2):
                    split_product(K.proj[j][:], (A.w_hi[:, j], A.w_lo[:, j]), (A.yhi[:], A.ylo[:])).then_inc(S.a_q, 1)
                pe.wait_ge(S.a_kr, 1 + 8 * g)
                for t in range(4):
                    ts = slice(t * P, (t + 1) * P)
                    mm = split_product(K.sc[0][:, ts], (A.yhi[:, ts], A.ylo[:, ts]), (A.w_hi[:, 2], A.w_lo[:, 2]))
                mm.then_inc(S.a_v, 1)

                def key_values(s):
                    if s == 0:
                        pe.wait_ge(S.a_te, 1 + g)
                    else:
                        pe.wait_ge(S.a_x, 1 + g)
                    pe.wait_ge(S.a_vb, g + 1)
                    pe.wait_ge(S.a_ke, 8 * g + 4 * s + 4)
                    for m in range(A_M):
                        for u in range(2):
                            t = 2 * s + u
                            mm = pe.matmul(K.pt[s][:, m * 17:(m + 1) * 17], A.kp[:, t, m * P:(m + 1) * P], A.v[:, t, m],
                                           start=(u == 0), stop=(u == 1))
                    mm.then_inc(S.a_kv, 1)

                for x in range(8):
                    t, half = x // 2, x % 2
                    if x == 0:
                        pe.wait_ge(S.a_lo, 2 * g + 2)
                    elif x == 1:
                        pe.wait_ge(S.a_vb, g + 1)
                    else:
                        pe.wait_ge(S.a_kr, 1 + 8 * g + x - 1)
                    ts = slice(t * P, (t + 1) * P)
                    hs = slice(half * 512, (half + 1) * 512)
                    split_product(K.sc[(x + 1) % 2][:], (A.khi[:, ts], A.klo[:, ts]), (A.bd_hi[:, hs], A.bd_lo[:, hs])).then_inc(S.a_kp, 1)
                    if x >= 2:
                        pe.wait_ge(S.a_qe, 1 + 8 * g + x - 1)
                    ms = slice(x * P, (x + 1) * P)
                    split_product(K.proj[x % 2][:], (A.bd_hi[:, ms], A.bd_lo[:, ms]), (A.qhi[:], A.qlo[:])).then_inc(S.a_qp, 1)
                    if x == 5:
                        key_values(0)
                key_values(1)
                pe.wait_ge(S.a_qe, 1 + 8 * g + 8)
                for s in range(2):
                    bank = (K.ss, K.ob)[s]
                    pe.wait_ge(S.a_on, 1 + 2 * g + s)
                    pe.wait_ge(S.a_bd, 8 * g + 4 * s + 4)
                    for u in range(2):
                        for m in range(A_M):
                            t = 2 * s + u
                            o = u * A_M * A_OUT + m * A_OUT
                            mm = pe.matmul(bank[:, o:o + A_OUT], A.qp[:, m, t * P:(t + 1) * P], A.kvbd[:, s, m],
                                           start=True, stop=True)
                    mm.then_inc(S.a_o, 1)
                pe.wait_ge(S.a_on, 1 + 2 * g + 2)
                for t in range(4):
                    mm = pe.transpose(K.pt[0][:, t * P:(t + 1) * P], A.on[:, t], K.ident[:])
                mm.then_inc(S.a_t, 1)
                pe.wait_ge(S.a_te, 1 + g + 1)
                pe.matmul(K.pt[1][:], A.w[:, 3], A.ot[:], start=True, stop=True).then_inc(S.a_w, 1)

        @block.scalar
        def _(act):
            with act.Fori(0, PAIRS) as g:
                for j in range(2):
                    act.wait_ge(S.a_q, 2 * g + j + 1)
                    if j == 0:
                        act.wait_ge(S.a_kp, 1 + 8 * g)
                        act.wait_ge(S.a_qp, 1 + 8 * g)
                    dst = (A.qhi, A.khi)[j]
                    act.activation(dst[:], K.proj[j][:], ACT.Identity, bias=A.b[:, j:j + 1]).then_inc(S.a_hi, 1)
                for x in range(8):
                    act.wait_ge(S.a_kp, 1 + 8 * g + x + 1)
                    if x == 0:
                        act.wait_ge(S.a_kv, 1 + 2 * g)
                    t, half = x // 2, x % 2
                    act.activation(A.kr[:, t, half * 512:(half + 1) * 512], K.sc[(x + 1) % 2][:], ACT.Relu).then_inc(S.a_kr, 1)
                act.wait_ge(S.a_t, 1 + g + 1)
                act.copy(A.ot[:], K.pt[0][:]).then_inc(S.a_te, 1)

        @block.gpsimd
        def _(pool):
            with pool.Fori(0, PAIRS) as g:
                for x in range(8):
                    t, half = x // 2, x % 2
                    hs = slice(half * 512, (half + 1) * 512)
                    pool.wait_ge(S.a_kr, 1 + 8 * g + x + 1)
                    pool.tensor_tensor(A.kp[:, t, hs], A.kr[:, t, hs], A.eps[:].broadcast_to([P, 512]), ALU.add).then_inc(S.a_ke, 1)

        @block.vector
        def _(dve):
            with dve.Fori(0, PAIRS) as g:
                sl = bass.ds(g * PAIR, PAIR)
                dve.wait_ge(S.a_v, 1 + g)
                dve.tensor_copy(A.yhi[:], K.HI[:, sl])
                dve.tensor_copy(A.ylo[:], K.LO[:, sl]).then_inc(S.a_yc, 1)
                for j in range(2):
                    hi, lo = ((A.qhi, A.qlo), (A.khi, A.klo))[j]
                    dve.wait_ge(S.a_hi, 2 * g + j + 1)
                    dve.scalar_tensor_tensor(lo[:], K.proj[j][:], A.b[:, j:j + 1], hi[:].bitcast(F32),
                                             ALU.add, ALU.subtract).then_inc(S.a_lo, 1)
                dve.wait_ge(S.a_v, 1 + g + 1)
                dve.wait_ge(S.a_kv, 1 + 2 * g)
                for t in range(4):
                    ins = dve.tensor_tensor(A.v[:, t, :, 0:16], K.sc[0][:, t * P:(t + 1) * P].rearrange("p (m d) -> p m d", d=16),
                                            A.bv[:].rearrange("p (m d) -> p m d", d=16), ALU.add)
                ins.then_inc(S.a_vb, 1)

                def diagonal(s):
                    dve.wait_ge(S.a_kv, 1 + 2 * g + s + 1)
                    if s == 0:
                        dve.wait_ge(S.a_o, 1 + 2 * g)
                    kv = K.pt[s][:, 0:A_M * 17].rearrange("p (m d) -> p m d", d=17)
                    for e in range(2):
                        r = slice(64 * e, 64 * e + 64)
                        dve.tensor_copy(A.kvbd[r, s, :, 8 * e:8 * e + 8], kv[r, :, 8 * e:8 * e + 8]).then_inc(S.a_bd, 1)
                        dve.tensor_copy(A.kvbd[r, s, :, 16 + e:17 + e], kv[r, :, 16:17]).then_inc(S.a_bd, 1)

                for m in range(A_M):
                    dve.wait_ge(S.a_qp, 1 + 8 * g + m + 1)
                    if m == 0:
                        dve.wait_ge(S.a_o, 1 + 2 * g)
                    dve.tensor_scalar(A.qp[:, m], K.proj[m % 2][:], 0.0, A_EPS, ALU.max, ALU.add).then_inc(S.a_qe, 1)
                    if m == 6:
                        diagonal(0)
                diagonal(1)
                for s in range(2):
                    bank = (K.ss, K.ob)[s][:, 0:2 * A_M * A_OUT].rearrange("p (a d) -> p a d", d=A_OUT)
                    dve.wait_ge(S.a_o, 1 + 2 * g + s + 1)
                    dve.wait_ge(S.a_rc, 1 + 2 * g + s)
                    dve.tensor_scalar(A.den[:, s].rearrange("p (a e) -> p a e", e=2), bank[:, :, 16:18], A_EPS, None, ALU.add).then_inc(S.a_dn, 1)
                    dve.wait_ge(S.a_dn, 2 * g + s + 1)
                    dve.wait_ge(S.a_on, 1 + 2 * g + s)
                    dve.reciprocal(A.rden[:, s], A.den[:, s]).then_inc(S.a_rc, 1)
                    dve.wait_ge(S.a_rc, 1 + 2 * g + s + 1)
                    if s == 0:
                        dve.wait_ge(S.a_t, 1 + g)
                    for e in range(2):
                        ins = dve.tensor_tensor(A.on[:, 2 * s:2 * s + 2].rearrange("p u (m e d) -> p (u m) e d", e=2, d=8)[:, :, e],
                                                bank[:, :, 8 * e:8 * e + 8],
                                                A.rden[:, s].rearrange("p (a e) -> p a e", e=2)[:, :, e:e + 1].broadcast_to([P, 16, 8]), ALU.mult)
                    ins.then_inc(S.a_on, 1)
                dve.wait_ge(S.a_w, g + 1)
                dve.scalar_tensor_tensor(K.X[:, sl], K.pt[1][:], A.b[:, 2:3], K.X[:, sl], ALU.add, ALU.add).then_inc(S.a_x, 1)


B_HEADS, B_G, B_DH = 16, 16, 8
B_T = SEQ // B_HEADS
RING = 4
KH_PIECES = 4
B_SCALE = float(np.float32(1.0 / np.sqrt(DIM)))


def column_attention_block(nc, K, B):
    S = K.s
    d = K.d
    score_banks = (K.proj[0], K.proj[1], K.sc[0], K.sc[1])

    with nc.Block() as block:
        @block.gpsimd
        def _(pool):
            pool.memset(B.qs[:].bitcast(F32), 0.0)
            pool.memset(B.kh[:].bitcast(F32), 0.0)

        @block.sync
        def _(sp):
            for k, name in enumerate(("Wq", "Wk", "Wv", "Wo")):
                sp.dma_start(B.w[:, k], d["L0_attn_b_" + name]).then_inc(S.b_in, 16)
            for k, name in enumerate(("bq", "bk", "bv", "bo")):
                sp.dma_start(B.b[:, k:k + 1], d["L0_attn_b_" + name].rearrange("(p o) -> p o", o=1)).then_inc(S.b_in, 16)

        @block.vector
        def _(dve):
            dve.wait_ge(S.b_in, 16 * 8)
            dve.tensor_copy(B.w_hi[:], B.w[:, 0:3]).then_inc(S.b_whi, 1)
            dve.tensor_scalar(B.bs[:], B.b[:, 0:2], B_SCALE, None, ALU.mult)
            dve.wait_ge(S.b_whi, 1)
            dve.tensor_tensor(B.w_lo[:], B.w[:, 0:3], B.w_hi[:].bitcast(F32), ALU.subtract)

    with nc.Block() as block:
        @block.tensor
        def _(pe):
            with pe.Fori(0, PAIRS) as g:
                sl = bass.ds(g * PAIR, PAIR)
                for j in range(3):
                    bank = (K.proj[0], K.proj[1], K.sc[0])[j]
                    pe.wait_ge(S.b_full, 1 + 3 * g + j)
                    pe.matmul(bank[:], B.w_hi[:, j], K.HI[:, sl], start=True, stop=False)
                    pe.matmul(bank[:], B.w_hi[:, j], K.LO[:, sl], start=False, stop=False)
                    pe.matmul(bank[:], B.w_lo[:, j], K.HI[:, sl], start=False, stop=True).then_inc(S.b_proj, 1)

        @block.vector
        def _(dve):
            with dve.Fori(0, PAIRS) as g:
                sl = bass.ds(g * PAIR, PAIR)
                for j in range(2):
                    dve.wait_ge(S.b_proj, 3 * g + j + 1)
                    dve.wait_ge(S.b_lo, 1 + 2 * g + j)
                    dve.tensor_scalar(B.full[:, j], K.proj[j][:], B_SCALE, B.bs[:, j:j + 1], ALU.mult, ALU.add).then_inc(S.b_full, 1)
                dve.wait_ge(S.b_proj, 3 * g + 3)
                dve.tensor_scalar(K.Y[:, sl], K.sc[0][:], B.b[:, 2:3], None, ALU.add).then_inc(S.b_full, 1)

        @block.scalar
        def _(act):
            with act.Fori(0, PAIRS) as g:
                for j in range(2):
                    act.wait_ge(S.b_full, 1 + 3 * g + j + 1)
                    act.wait_ge(S.b_out, 1 + 64 * g)
                    act.copy(B.hi[:, j], B.full[:, j]).then_inc(S.b_hi, 1)

        @block.gpsimd
        def _(pool):
            with pool.Fori(0, PAIRS) as g:
                for j in range(2):
                    pool.wait_ge(S.b_hi, 2 * g + j + 1)
                    pool.tensor_tensor(B.lo[:, j], B.full[:, j], B.hi[:, j].bitcast(F32), ALU.subtract).then_inc(S.b_lo, 1)

        @block.sync
        def _(sp):
            with sp.Fori(0, PAIRS) as g:
                sl = bass.ds(g * PAIR, PAIR)
                for j in range(2):
                    sp.wait_ge(S.b_lo, 1 + 2 * g + j + 1)
                    sp.dma_start(B.scr[2 * j, :, sl], B.hi[:, j].bitcast(F32)).then_inc(S.b_out, 16)
                    sp.dma_start(B.scr[2 * j + 1, :, sl], B.lo[:, j].bitcast(F32)).then_inc(S.b_out, 16)
            sp.wait_ge(S.b_out, 1 + 64 * PAIRS)

    with nc.Block() as block:
        @block.sync
        def _(sp):
            def load(q, s):
                for r in range(4):
                    rows = slice(r * B_DH, (r + 1) * B_DH)
                    for dst, part in ((B.qs[rows, s], r % 2), (B.ks[rows], 2 + r // 2)):
                        sp.dma_start(dst.bitcast(F32), B.scr[part, :, bass.ds(q * SEQ, SEQ)].rearrange(
                            "(g x) t -> x g t", x=B_DH)).then_inc(S.b_ld, 16)

            sp.dma_start(B.scr[:, :, TOK:TOK + PAIR], B.scr[:, :, 0:PAIR]).then_inc(S.b_wrap, 16)
            load(0, 0)
            sp.wait_ge(S.b_kh, KH_PIECES)
            load(1, 1)
            sp.wait_ge(S.b_wrap, 16)
            with sp.Fori(0, PAIRS) as g:
                for s in range(2):
                    q = 2 * g + s
                    sp.wait_ge(S.b_rt, q + 1)
                    sp.dma_start(B.rscr[bass.ds(q, 1)].rearrange("a (e h) n -> (a e h) n", h=2), B.rt).then_inc(S.b_st, 16)
                    load(q + 2, s)
            sp.wait_ge(S.b_st, 1 + 16 * SEQS)
            sp.wait_ge(S.b_ld, 128 * (SEQS + 2))

        @block.tensor
        def _(pe):
            with pe.Fori(0, PAIRS) as g:
                for s in range(2):
                    q = 2 * g + s
                    pe.wait_ge(S.b_kh, KH_PIECES * (q + 1))

                    def row_sums(e):
                        pe.wait_ge(S.b_rd, 16 * q + e + 1)
                        if e == 0 and s == 0:
                            pe.wait_ge(S.b_rc, 1 + 2 * g)
                        elif e == 0:
                            pe.wait_ge(S.b_rc, 1 + 2 * g + 1)
                        for ah in range(2):
                            for bt in range(2):
                                mm = pe.matmul(K.ss[:, 2 * e + ah:2 * e + ah + 1],
                                               B.E[:, e % RING, bt, ah * P:(ah + 1) * P], B.rd[:, e % RING, bt:bt + 1],
                                               start=(bt == 0), stop=(bt == 1))
                        mm.then_inc(S.b_rs, 1)

                    for e in range(B_HEADS):
                        es = slice(e * B_T, (e + 1) * B_T)
                        if e >= RING:
                            pe.wait_ge(S.b_ex, 1 + 32 * q + 2 * (e - RING + 1))
                        else:
                            pe.wait_ge(S.b_ex, 1 + 32 * q)
                        bank = score_banks[e % RING]
                        for bt in range(2):
                            mm = pe.matmul(bank[:, bt * SEQ:(bt + 1) * SEQ],
                                           B.kh[:, s, e, bt * P:(bt + 1) * P], B.qs[:, s, :, es], start=True, stop=True)
                        mm.then_inc(S.b_sc, 1)
                        if e >= RING - 1:
                            row_sums(e - RING + 1)
                    for e in range(B_HEADS - RING + 1, B_HEADS):
                        row_sums(e)
                    pe.wait_ge(S.b_rc, 1 + q + 1)
                    pe.transpose(K.pt[0][0:32, 0:P], B.r[:], K.ident[:]).then_inc(S.b_tr, 1)

        @block.vector
        def _(dve):
            def reorder(q, s, piece):
                es = slice(piece * B_HEADS // KH_PIECES, (piece + 1) * B_HEADS // KH_PIECES)
                if piece == 0:
                    dve.wait_ge(S.b_ld, 128 * (q + 1))
                dve.tensor_copy(B.kh[0:4 * B_DH, s, es].rearrange("p e (g t) -> p e g t", t=B_T),
                                B.ks[0:4 * B_DH].rearrange("p g (e t) -> p e g t", t=B_T)[:, es]).then_inc(S.b_kh, 1)

            for piece in range(KH_PIECES):
                reorder(0, 0, piece)
            with dve.Fori(0, PAIRS) as g:
                for s in range(2):
                    q = 2 * g + s

                    def inverse(e):
                        dve.wait_ge(S.b_ex, 1 + 32 * q + 2 * e + 2)
                        if e >= RING:
                            dve.wait_ge(S.b_rs, 16 * q + e - RING + 1)
                        dve.reciprocal(B.rd[:, e % RING], B.dn[:, e % RING]).then_inc(S.b_rd, 1)

                    for e in range(B_HEADS):
                        dve.wait_ge(S.b_sc, 1 + 16 * q + e + 1)
                        dve.tensor_reduce(B.nm[:, e % RING], score_banks[e % RING][:].rearrange("p (b a) -> p b a", b=2),
                                          AX.X, ALU.max, negate=True).then_inc(S.b_mx, 1)
                        if e >= 2:
                            inverse(e - 2)
                        if e % 2 == 0 and 4 <= e < 4 + 2 * KH_PIECES:
                            reorder(q + 1, 1 - s, e // 2 - 2)
                    inverse(B_HEADS - 2)
                    inverse(B_HEADS - 1)
                    dve.wait_ge(S.b_rs, 16 * q + 16)
                    dve.wait_ge(S.b_tr, 1 + q)
                    dve.tensor_copy(B.r[:], K.ss[:, 0:32]).then_inc(S.b_rc, 1)
                    dve.wait_ge(S.b_tr, 1 + q + 1)
                    dve.wait_ge(S.b_st, 1 + 16 * q)
                    dve.tensor_copy(B.rt, K.pt[0][0:32, 0:P]).then_inc(S.b_rt, 1)

        @block.scalar
        def _(act):
            act.preload_act_table_set("exp_and_others")
            with act.Fori(0, PAIRS) as g:
                for s in range(2):
                    q = 2 * g + s
                    for e in range(B_HEADS):
                        act.wait_ge(S.b_mx, 16 * q + e + 1)
                        if e >= RING:
                            act.wait_ge(S.b_rs, 16 * q + e - RING + 1)
                        for bt in range(2):
                            act.activation(B.E[:, e % RING, bt], score_banks[e % RING][:, bt * SEQ:(bt + 1) * SEQ], ACT.Exp,
                                           bias=B.nm[:, e % RING, bt:bt + 1], accum_out=B.dn[:, e % RING, bt:bt + 1]).then_inc(S.b_ex, 1)

    with nc.Block() as block:
        @block.sync
        def _(sp):
            src = B.rscr.rearrange("q (e h) (k t) -> (h k) q e t", h=2, t=B_T)
            for gr in range(B_G):
                sp.dma_start(B.R[gr * B_DH:(gr + 1) * B_DH].rearrange("p (a t) -> p a t", t=B_T),
                             src[gr].rearrange("q e t -> (q e) t").partition_broadcast(B_DH)).then_inc(S.b_r, 16)

        @block.gpsimd
        def _(pool):
            pool.wait_ge(S.b_r, 16 * B_G)
            with pool.Fori(0, PAIRS) as g:
                sl = bass.ds(g * PAIR, PAIR)
                pool.wait_ge(S.b_wo, 1 + g)
                pool.tensor_tensor(B.o, B.R[:, sl], K.Y[:, sl], ALU.mult).then_inc(S.b_o, 1)

        @block.tensor
        def _(pe):
            with pe.Fori(0, PAIRS) as g:
                pe.wait_ge(S.b_o, g + 1)
                pe.wait_ge(S.b_x, 1 + g)
                pe.matmul(K.ob[:], B.w[:, 3], B.o, start=True, stop=True).then_inc(S.b_wo, 1)

        @block.vector
        def _(dve):
            with dve.Fori(0, PAIRS) as g:
                sl = bass.ds(g * PAIR, PAIR)
                dve.wait_ge(S.b_wo, 1 + g + 1)
                dve.scalar_tensor_tensor(K.X[:, sl], K.ob[:], B.b[:, 3:4], K.X[:, sl], ALU.add, ALU.add).then_inc(S.b_x, 1)


class Semaphores:

    def __init__(self, new):
        self.const_in = new("const_in")
        self.x_in = new("x_in")
        self.xt_done = new("xt_done")
        self.xt_out = new("xt_out")
        self.fin_sum = new("fin_sum")
        self.fin_t = new("fin_t")
        self.fin_out = new("fin_out")
        self.stored = new("stored")
        self.ln_src = new("ln_src")
        self.ln_mean = new("ln_mean")
        self.ln_cent = new("ln_cent")
        self.ln_sq = new("ln_sq")
        self.ln_var = new("ln_var")
        self.ln_log = new("ln_log")
        self.ln_rstd = new("ln_rstd")
        self.ln_nrm = new("ln_nrm")
        self.ln_aff = new("ln_aff")
        self.ln_hi = new("ln_hi")
        self.w_in = new("w_in")
        self.w_hi = new("w_hi")
        self.h_hi = new("h_hi")
        self.h_lo = new("h_lo")
        self.proj = new("proj")
        self.v_out = new("v_out")
        self.sq = new("sq")
        self.prod = new("prod")
        self.k_rot = new("k_rot")
        self.q_rot = new("q_rot")
        self.scores = new("scores")
        self.mx = new("mx")
        self.ex = new("ex")
        self.ss = new("ss")
        self.ln_ss = new("ln_ss")
        self.rn = new("rn")
        self.rsum = new("rsum")
        self.ptd = new("ptd")
        self.pt_act = new("pt_act")
        self.pt_dve = new("pt_dve")
        self.pv = new("pv")
        self.rden = new("rden")
        self.onorm = new("onorm")
        self.wo = new("wo")
        self.y_upd = new("y_upd")
        self.up = new("up")
        self.gl = new("gl")
        self.u = new("u")
        self.dn = new("dn")
        self.ff_y = new("ff_y")
        self.a_zero = new("a_zero")
        self.a_in = new("a_in")
        self.a_whi = new("a_whi")
        self.a_yc = new("a_yc")
        self.a_q = new("a_q")
        self.a_hi = new("a_hi")
        self.a_lo = new("a_lo")
        self.a_v = new("a_v")
        self.a_vb = new("a_vb")
        self.a_kp = new("a_kp")
        self.a_kr = new("a_kr")
        self.a_ke = new("a_ke")
        self.a_qp = new("a_qp")
        self.a_qe = new("a_qe")
        self.a_kv = new("a_kv")
        self.a_bd = new("a_bd")
        self.a_o = new("a_o")
        self.a_dn = new("a_dn")
        self.a_rc = new("a_rc")
        self.a_on = new("a_on")
        self.a_t = new("a_t")
        self.a_te = new("a_te")
        self.a_w = new("a_w")
        self.a_x = new("a_x")
        self.b_in = new("b_in")
        self.b_whi = new("b_whi")
        self.b_full = new("b_full")
        self.b_proj = new("b_proj")
        self.b_lo = new("b_lo")
        self.b_hi = new("b_hi")
        self.b_out = new("b_out")
        self.b_ld = new("b_ld")
        self.b_wrap = new("b_wrap")
        self.b_kh = new("b_kh")
        self.b_sc = new("b_sc")
        self.b_ex = new("b_ex")
        self.b_rd = new("b_rd")
        self.b_rc = new("b_rc")
        self.b_rs = new("b_rs")
        self.b_tr = new("b_tr")
        self.b_mx = new("b_mx")
        self.b_st = new("b_st")
        self.b_rt = new("b_rt")
        self.b_r = new("b_r")
        self.b_o = new("b_o")
        self.b_wo = new("b_wo")
        self.b_x = new("b_x")
        self.primed = (self.ln_cent, self.ln_nrm, self.prod, self.proj, self.ln_ss, self.pt_act, self.pt_dve,
                       self.y_upd, self.ff_y, self.a_qe, self.a_kr, self.a_te, self.a_x, self.a_on, self.a_kp,
                       self.a_qp, self.a_kv, self.a_v, self.a_o, self.a_rc, self.a_t, self.b_full, self.b_lo,
                       self.b_out, self.b_sc, self.b_ex, self.b_rc, self.b_tr, self.b_st, self.b_wo, self.b_x)




class Bag:
    pass




def ffn(nc, K, rep):
    with ExitStack() as ctx:
        def sb(name, shape, dt=F32):
            return ctx.enter_context(nc.sbuf_tensor(f"ffn{rep}_" + name, shape, dt))

        K.wqk_hi = sb("wqk_hi", [P, 4, INNER], F32R)
        K.wqk_lo = sb("wqk_lo", [P, 4, INNER], F32R)
        K.wv_hi = sb("wv_hi", [P, INNER], F32R)
        K.wv_lo = sb("wv_lo", [P, INNER], F32R)
        K.w1_hi = sb("w1_hi", [P, 2 * HID], F32R)
        K.w1_lo = sb("w1_lo", [P, 2 * HID], F32R)
        K.wo = sb("wo", [P, CHUNKS, P])
        K.w2 = sb("w2", [P, 3, P])
        K.colb = sb("colb", [P, 6])
        K.cols = sb("cols", [P, 4])
        K.tab = sb("tab", [P, 4, SEQ])
        K.hhi = sb("hhi", [P, PAIR], F32R)
        K.hlo = sb("hlo", [P, PAIR], F32R)
        K.v = sb("v", [P, 4, INNER])
        K.sqb = sb("sqb", [P, 2, PAIR])
        K.lss = sb("lss", [P, 2, PAIR])
        K.qrot = sb("qrot", [P, 2, PAIR])
        K.kpad = sb("kpad", [P, 2, 2, PAIR])
        K.nmax = sb("nmax", [P, 2, 8])
        K.den = sb("den", [P, 2, 8])
        K.rden = sb("rden", [P, 2, 8])
        K.p0 = sb("p0", [P, 2, 4, P])
        K.p1 = sb("p1", [P, 2, 4, SEQ])
        K.ptb = sb("ptb", [P, 2, 3, 4, P])
        K.on = sb("on", [P, 2, 4, P])
        K.ot = sb("ot", [P, CHUNKS, PAIR])
        K.stage = K.v[:].rearrange("p a b -> p (a b)")
        K.stage1 = K.ot[:].rearrange("p a b -> p (a b)")[:, 0:2 * HID]
        with nc.Block() as block:
            @block.gpsimd
            def _(pool):
                pool.memset(K.kpad[:], 0.0)
                pool.memset(K.p1[:], 0.0)
                pool.memset(K.hhi[:].bitcast(F32), 0.0)
                pool.memset(K.hlo[:].bitcast(F32), 0.0)
        with nc.Fori(0, DEPTH) as l:
            n = rep * DEPTH + l
            weights_block(nc, K, l, n)
            attention_block(nc, K, n)
            K.aff_n = n
            K.split_n = n + 1 + rep
            norm_block(nc, K, n + 2 + 2 * rep, shift=True, affine=True, split=True)
            geglu_block(nc, K, n)


def linear_attention(nc, K):
    with ExitStack() as ctx:
        def sb(name, shape, dt=F32):
            return ctx.enter_context(nc.sbuf_tensor("linear_" + name, shape, dt))

        A = Bag()
        A.w = sb("w", [P, 4, P])
        A.b = sb("b", [P, 3])
        A.eps = sb("eps", [P, 1])
        A.bv = sb("bv", [P, P])
        A.bd = sb("bd", [P, A_FEAT])
        A.w_hi = sb("w_hi", [P, 3, P], F32R)
        A.w_lo = sb("w_lo", [P, 3, P], F32R)
        A.bd_hi = sb("bd_hi", [P, A_FEAT], F32R)
        A.bd_lo = sb("bd_lo", [P, A_FEAT], F32R)
        A.yhi = sb("yhi", [P, PAIR], F32R)
        A.ylo = sb("ylo", [P, PAIR], F32R)
        A.qhi = sb("qhi", [P, PAIR], F32R)
        A.qlo = sb("qlo", [P, PAIR], F32R)
        A.khi = sb("khi", [P, PAIR], F32R)
        A.klo = sb("klo", [P, PAIR], F32R)
        A.v = sb("v", [P, 4, A_M, 17])
        A.kr = sb("kr", [P, 4, A_FEAT])
        A.kp = sb("kp", [P, 4, A_FEAT])
        A.qp = sb("qp", [P, A_M, PAIR])
        A.kvbd = sb("kvbd", [P, 2, A_M, A_OUT])
        A.den = sb("den", [P, 2, 32])
        A.rden = sb("rden", [P, 2, 32])
        A.on = sb("on", [P, 4, P])
        A.ot = sb("ot", [P, PAIR])
        linear_attention_block(nc, K, A)


def column_attention(nc, K):
    with ExitStack() as ctx:
        def sb(name, shape, dt=F32):
            return ctx.enter_context(nc.sbuf_tensor("column_" + name, shape, dt))

        B = Bag()
        B.w = sb("w", [P, 4, P])
        B.b = sb("b", [P, 4])
        B.bs = sb("bs", [P, 2])
        B.w_hi = sb("w_hi", [P, 3, P], F32R)
        B.w_lo = sb("w_lo", [P, 3, P], F32R)
        B.full = sb("full", [P, 2, PAIR])
        B.hi = sb("hi", [P, 2, PAIR], F32R)
        B.lo = sb("lo", [P, 2, PAIR], F32R)
        B.qs = sb("qs", [P, 2, B_G, SEQ], F32R)
        B.ks = sb("ks", [P, B_G, SEQ], F32R)
        B.kh = sb("kh", [P, 2, B_HEADS, SEQ], F32R)
        B.E = sb("E", [P, RING, 2, SEQ])
        B.nm = sb("nm", [P, RING, 2])
        B.dn = sb("dn", [P, RING, 2])
        B.rd = sb("rd", [P, RING, 2])
        B.r = sb("r", [P, 32])
        B.rt = B.full[0:32, 1, 0:P]
        B.o = B.full[:, 0]
        B.R = K.HI[:].bitcast(F32)
        B.scr = nc.dram_tensor("qk_parts", [4, P, TOK + PAIR], F32, kind="Internal").ap()
        B.rscr = nc.dram_tensor("row_sums", [SEQS, 2 * B_HEADS, P], F32, kind="Internal").ap()
        column_attention_block(nc, K, B)


def build(nc, d, out):
    with ExitStack() as ctx:
        K = Bag()
        K.d, K.out = d, out
        K.s = Semaphores(lambda name: ctx.enter_context(nc.semaphore(name)))

        def sb(name, shape, dt=F32):
            return ctx.enter_context(nc.sbuf_tensor(name, shape, dt))

        def ps(name):
            return ctx.enter_context(nc.psum_tensor(name, [P, 512], F32))

        K.X = sb("X", [P, TOK])
        K.Y = sb("Y", [P, TOK])
        K.HI = sb("HI", [P, TOK], F32R)
        K.LO = sb("LO", [P, TOK], F32R)
        K.tok = K.Y[:].rearrange("p (j c) -> p j c", c=P)
        K.ident = sb("ident", [P, P])
        K.identb = sb("identb", [P, P], BF16)
        K.rot = sb("rot", [P, 4, SEQ])
        K.mask = sb("mask", [P, P + 192], BF16)
        K.mean_w = sb("mean_w", [P, P])
        K.head_w = sb("head_w", [P, P])
        K.eps = sb("eps", [P, 1])
        K.ssb = sb("ssb", [P, 1])
        K.rsb = sb("rsb", [P, 1])
        K.colp = sb("colp", [P, 3])
        K.rn = sb("rn", [P, 2, 2, PAIR])
        K.pa = sb("pa", [P, 2, 2, PAIR])
        K.pb = sb("pb", [P, 2, 2, PAIR])
        K.rsum = sb("rsum", [P, 2, 2, PAIR])
        K.lns, K.lnd, K.lnq, K.lnl, K.lnr, K.lnf, K.lng = (
            K.pa[:, 0], K.pa[:, 1], K.pb[:, 0], K.pb[:, 1], K.rsum[:, 0], K.rsum[:, 1], K.rn[:, 0])
        K.gl = K.pa[:, 0]
        K.u = K.pb[:, 0]
        K.proj = [ps("proj0"), ps("proj1")]
        K.sc = [ps("sc0"), ps("sc1")]
        K.pt = [ps("pt0"), ps("pt1")]
        K.ss, K.ob = ps("ss"), ps("ob")

        load_block(nc, K)
        K.split_n = 0
        norm_block(nc, K, 0, split=True)
        linear_attention(nc, K)
        norm_block(nc, K, 1)
        ffn(nc, K, 0)
        K.split_n = 1 + DEPTH
        norm_block(nc, K, 2 + DEPTH, add_y=True, split=True)
        column_attention(nc, K)
        norm_block(nc, K, 3 + DEPTH)
        ffn(nc, K, 1)
        store_block(nc, K)


OUT_SHAPE = (SEQS, SEQ, DIM)


def kernel(**inputs):
    import concourse.bacc as bacc
    from concourse.bass_utils import run_bass_kernel_spmd
    nc = bacc.Bacc("TRN2", target_bir_lowering=False, num_devices=1)
    arrays = {k: np.ascontiguousarray(v) for k, v in inputs.items()} | constants()
    d = {k: nc.dram_tensor(k, a.shape, mybir.dt.from_np(a.dtype), kind="ExternalInput").ap() for k, a in arrays.items()}
    out = nc.dram_tensor("out", OUT_SHAPE, F32, kind="ExternalOutput").ap()
    build(nc, d, out)
    r = run_bass_kernel_spmd(nc, [arrays], core_ids=[0])
    return r.results[0]["out"]
```
